# Optimizing a Trainium2 kernel written in Bass

```python
import numpy as np
import jax
import jax.numpy as jnp

def _softmax(x, axis=-1):
    return jax.nn.softmax(x, axis=axis)

def _gelu(x):
    return jax.nn.gelu(x, approximate=True)

def _silu(x):
    return jax.nn.silu(x)

def _sigmoid(x):
    return jax.nn.sigmoid(x)

def _layernorm(x, axis=-1, eps=1e-05):
    m = jnp.mean(x, axis=axis, keepdims=True)
    v = jnp.var(x, axis=axis, keepdims=True)
    return (x - m) / jnp.sqrt(v + eps)

def _scatter_add(tgt, idx, src, axis=0):
    return tgt.at[idx].add(src)

def _segment_sum(src, seg, n):
    return jax.ops.segment_sum(src, seg, n)
kernel_name = 'mk_gnn_resnorm_d2_gnn_r8_74b7f2'

def setup_inputs(seed: int=0):
    np.random.seed(seed)
    _w = jnp.asarray

    def _rec_inputs():
        import jax
        import jax.numpy as jnp
        _gk = jax.random.key(seed)
        x = -0.000202 + 1 * jax.random.normal(jax.random.fold_in(_gk, 1), (12500, 128), jnp.float32)
        src = jax.random.randint(jax.random.fold_in(_gk, 2), (400000,), 0, 12500, jnp.int32)
        dst = jax.random.randint(jax.random.fold_in(_gk, 3), (400000,), 0, 12500, jnp.int32)
        _o = jnp.argsort(dst, stable=True)
        src = src[_o]
        dst = dst[_o]
        edge_attr_64 = 0.000167468 + 1.0002 * jax.random.normal(jax.random.fold_in(_gk, 12), (400000, 64), jnp.float32)
        return (x, src, dst, edge_attr_64)
    x, src, dst, edge_attr_64 = _rec_inputs()

    def _L0_gnn_setup():
        import jax, jax.numpy as jnp
        import numpy as np
        N_NODES = 6250
        N_EDGES = 80000
        NODE_DIM = 128
        EDGE_DIM = 64
        HIDDEN_DIM = 128
        key = jax.random.key(seed)
        ks = jax.random.split(key, 12)
        x = jax.random.normal(ks[0], (N_NODES, NODE_DIM), dtype=jnp.float32)
        edge_index = jax.random.randint(ks[1], (2, N_EDGES), 0, N_NODES, dtype=jnp.int64)
        edge_attr = jax.random.normal(ks[2], (N_EDGES, EDGE_DIM), dtype=jnp.float32)
        fan1 = NODE_DIM + EDGE_DIM
        W1 = jax.random.normal(ks[3], (HIDDEN_DIM, fan1), dtype=jnp.float32) / np.sqrt(fan1)
        b1 = jnp.zeros((HIDDEN_DIM,), dtype=jnp.float32)
        W2 = jax.random.normal(ks[4], (HIDDEN_DIM, HIDDEN_DIM), dtype=jnp.float32) / np.sqrt(HIDDEN_DIM)
        b2 = jnp.zeros((HIDDEN_DIM,), dtype=jnp.float32)
        Wih = jax.random.normal(ks[5], (3 * NODE_DIM, HIDDEN_DIM), dtype=jnp.float32) / np.sqrt(HIDDEN_DIM)
        bih = jnp.zeros((3 * NODE_DIM,), dtype=jnp.float32)
        Whh = jax.random.normal(ks[6], (3 * NODE_DIM, NODE_DIM), dtype=jnp.float32) / np.sqrt(NODE_DIM)
        bhh = jnp.zeros((3 * NODE_DIM,), dtype=jnp.float32)
        return {'x': x, 'edge_index': edge_index, 'edge_attr': edge_attr, 'W1': W1, 'b1': b1, 'W2': W2, 'b2': b2, 'Wih': Wih, 'bih': bih, 'Whh': Whh, 'bhh': bhh}
    _L0_gnn_all = _L0_gnn_setup()
    _L0_gnn_in = {k: v for k, v in _L0_gnn_all.items() if k in ('W1', 'b1', 'W2', 'b2', 'Wih', 'bih', 'Whh', 'bhh')}
    del _L0_gnn_all

    def _L1_gnn_setup():
        import jax, jax.numpy as jnp
        import numpy as np
        N_NODES = 12500
        N_EDGES = 200000
        C_IN = 128
        C_OUT = 128
        key = jax.random.key(seed)
        k1, k2, k3, k4, k5 = jax.random.split(key, 5)
        x = jax.random.normal(k1, (N_NODES, C_IN), dtype=jnp.float32)
        weight = jax.random.normal(k2, (C_IN, C_OUT), dtype=jnp.float32) * (1.0 / np.sqrt(C_IN))
        root_weight = jax.random.normal(k3, (C_IN, C_OUT), dtype=jnp.float32) * (1.0 / np.sqrt(C_IN))
        bias = jnp.zeros((C_OUT,), dtype=jnp.float32)
        row = jax.random.randint(k4, (N_EDGES,), 0, N_NODES, dtype=jnp.int32)
        col = jax.random.randint(k5, (N_EDGES,), 0, N_NODES, dtype=jnp.int32)
        return {'x': x, 'weight': weight, 'root_weight': root_weight, 'bias': bias, 'row': row, 'col': col}
    _L1_gnn_all = _L1_gnn_setup()
    _L1_gnn_in = {k: v for k, v in _L1_gnn_all.items() if k in ('weight', 'root_weight', 'bias')}
    del _L1_gnn_all
    return {'x': x, 'src': src, 'dst': dst, 'edge_attr_64': edge_attr_64, 'L0_gnn_W1': _L0_gnn_in['W1'], 'L0_gnn_b1': _L0_gnn_in['b1'], 'L0_gnn_W2': _L0_gnn_in['W2'], 'L0_gnn_b2': _L0_gnn_in['b2'], 'L0_gnn_Wih': _L0_gnn_in['Wih'], 'L0_gnn_bih': _L0_gnn_in['bih'], 'L0_gnn_Whh': _L0_gnn_in['Whh'], 'L0_gnn_bhh': _L0_gnn_in['bhh'], 'L1_gnn_weight': _L1_gnn_in['weight'], 'L1_gnn_root_weight': _L1_gnn_in['root_weight'], 'L1_gnn_bias': _L1_gnn_in['bias']}

def reference(x, src, dst, edge_attr_64, L0_gnn_W1, L0_gnn_b1, L0_gnn_W2, L0_gnn_b2, L0_gnn_Wih, L0_gnn_bih, L0_gnn_Whh, L0_gnn_bhh, L1_gnn_weight, L1_gnn_root_weight, L1_gnn_bias):
    import jax
    import jax.numpy as jnp

    def _L0_gnn_ref(x, edge_index, edge_attr, W1, b1, W2, b2, Wih, bih, Whh, bhh):
        import jax, jax.numpy as jnp
        import numpy as np
        N_NODES = 6250
        N_EDGES = 80000
        NODE_DIM = 128
        EDGE_DIM = 64
        HIDDEN_DIM = 128
        src, dst = (edge_index[0], edge_index[1])
        msg_in = jnp.concatenate([x[src], edge_attr], axis=-1)
        h = jax.nn.relu(msg_in @ W1.T + b1)
        messages = h @ W2.T + b2
        agg = jax.ops.segment_sum(messages, dst, num_segments=x.shape[0])
        gi = agg @ Wih.T + bih
        gh = x @ Whh.T + bhh
        i_r, i_z, i_n = jnp.split(gi, 3, axis=-1)
        h_r, h_z, h_n = jnp.split(gh, 3, axis=-1)
        r = jax.nn.sigmoid(i_r + h_r)
        z = jax.nn.sigmoid(i_z + h_z)
        n = jnp.tanh(i_n + r * h_n)
        return (1.0 - z) * n + z * x

    def _L1_gnn_ref(x, weight, root_weight, bias, row, col):
        import jax, jax.numpy as jnp
        import numpy as np
        N_NODES = 12500
        N_EDGES = 200000
        C_IN = 128
        C_OUT = 128
        n = x.shape[0]
        agg = jax.ops.segment_sum(x[col], row, num_segments=n)
        deg = jax.ops.segment_sum(jnp.ones_like(row, dtype=x.dtype), row, num_segments=n)
        mean = agg / jnp.maximum(deg, 1.0)[:, None]
        return mean @ weight + x @ root_weight + bias
    edge_index = jnp.stack([src, dst])
    x = _layernorm(x + _L0_gnn_ref(x, edge_index, edge_attr_64, L0_gnn_W1, L0_gnn_b1, L0_gnn_W2, L0_gnn_b2, L0_gnn_Wih, L0_gnn_bih, L0_gnn_Whh, L0_gnn_bhh), axis=-1)
    x = _layernorm(x + _L1_gnn_ref(x, L1_gnn_weight, L1_gnn_root_weight, L1_gnn_bias, src, dst), axis=-1)
    return x

_drawn_inputs = setup_inputs


def setup_inputs(seed=0):
    import zlib

    import numpy as np

    out = dict(_drawn_inputs(seed))
    spreads = {'L0_gnn_b1': (0.0, 0.1),
     'L0_gnn_b2': (0.0, 0.1),
     'L0_gnn_bih': (0.0, 0.761),
     'L0_gnn_bhh': (0.0, 0.8),
     'L1_gnn_bias': (0.0, 0.1)}
    factors = {}
    for name, (base, spread) in spreads.items():
        noise = np.random.default_rng([zlib.crc32(name.encode()), seed]).standard_normal(out[name].shape)
        drawn = base * np.exp(spread * noise) if base else spread * noise
        out[name] = jnp.asarray(drawn.astype(out[name].dtype))
    for name, factor in factors.items():
        out[name] = (out[name] * factor).astype(out[name].dtype)
    return out
```

```python
from contextlib import ExitStack

import concourse.bass as bass
from concourse import mybir

fp32 = mybir.dt.float32
fp16 = mybir.dt.float16
int32 = mybir.dt.int32
ALU = mybir.AluOpType
ACT = mybir.ActivationFunctionType
AX = mybir.AxisListType

NODES, EDGES, D, DE = 12500, 400000, 128, 64
P = 128
TILES = EDGES // P
BT = 5
BLOCKS = TILES // BT
BE = BT * P
SEGW = 32
GN = 4
GPB = NODES // GN // BLOCKS
GROUPS = GPB * BLOCKS
CH = 32
LO = 392
NP = CH * LO
GP = NP // GN
W = NP // P
GR = P // GN
STEP = 32
KT = 2
KS = P // STEP
KW = EDGES // STEP
KP = 8
KC = (KW + KS + KP) // KP
KWP = KC * KP
NOEDGE = 16383
SAMP = 100
SR = KW // SAMP
SCALE = 2048.0
WB = 7
NB = W // WB
AW = 14
AL = W // AW
SJ, SM = 4, LO // 4
EPS = 1e-5
UN = 4
PEEL = 5
LATE = 2
ROUNDS = (BLOCKS - PEEL) // UN
assert PEEL + ROUNDS * UN == BLOCKS and GROUPS * GN == NODES and W * P == NP and NB * WB == W and AL * AW == W
assert KWP >= KW + KS and SR * SAMP == KW


class Place:

    def __init__(self, nc, ctx, phase=""):
        self.nc, self.ctx, self.prefix = nc, ctx, phase + "_" if phase else ""

    def sb(self, name, shape, dt=fp32):
        return self.ctx.enter_context(self.nc.sbuf_tensor(self.prefix + name, shape, dt))

    def ps(self, name, cols=512):
        return self.ctx.enter_context(self.nc.psum_tensor(self.prefix + name, [P, cols], fp32))

    def sem(self, name):
        return self.ctx.enter_context(self.nc.semaphore(self.prefix + name))

    def sems(self, name, n):
        return [self.sem(f"{name}{k}") for k in range(n)]


class Shared:
    pass


def reach(eng, sem, value):
    if not isinstance(value, int) or value > 0:
        eng.wait_ge(sem, value)


class Step:

    def __init__(self, i, c, un=UN):
        self.i, self.c, self.un = i, c, un

    def times(self, n, plus=0):
        return self.i * (n * self.un) + (n * self.c + plus)

    def turn(self, ring, n, back=0):
        return self.i * (n * (self.un // ring)) + n * (self.c // ring + 1 - back)

    def back(self, n):
        return Step(self.i, self.c - n, self.un)


def edge_loop(eng, body, opening=None):
    for c in range(PEEL):
        if opening:
            opening(Step(0, c), 1, c)
        body(Step(0, c))
    with eng.Fori(0, ROUNDS) as i:
        if opening:
            opening(Step(i, PEEL), UN, i + PEEL)
        for k in range(UN):
            body(Step(i, PEEL + k))


def wide(ap, n):
    return ap.unsqueeze(2).broadcast_to([ap.shape[0], ap.shape[1], n])


def tall(ap, m):
    return ap.unsqueeze(1).broadcast_to([ap.shape[0], m, ap.shape[1]])


def prologue(nc, h):
    NT = WB
    TC = NT * P
    NC = NP // TC
    halves_of = [(0, 4), (4, NT)]
    with ExitStack() as ctx:
        m = Place(nc, ctx, "prologue")
        xt = [m.sb(f"xt{k}", [D, TC]) for k in range(2)]
        ysb = [m.sb(f"ysb{k}", [P, NT, D]) for k in range(2)]
        w1a = m.sb("w1a", [D, D])
        b1b = m.sb("b1b", [P, D])
        samp = m.sb("samp", [SR, SAMP], int32)
        s_hi, s_lo = m.sb("s_hi", [SR, SAMP], int32), m.sb("s_lo", [SR, SAMP], int32)
        f_hi, f_lo = m.sb("f_hi", [SR, SAMP], fp16), m.sb("f_lo", [SR, SAMP], fp16)
        upper = m.sb("upper", [W, W])
        hist, cum, zrow = m.sb("hist", [W, P]), m.sb("cum", [W, P]), m.sb("zrow", [W, P])
        before, less, prev = m.sb("before", [W, P]), m.sb("less", [W, P]), m.sb("prev", [W, 1])
        first = m.sb("first_sb", [W, P // GN], int32)
        dbase = m.sb("dbase", [P, BLOCKS], int32)
        inside = m.sb("inside", [P, TILES], fp16)
        held = m.sb("held", [P, TILES], fp16)
        zero = m.sb("zero", [P, (GP - GROUPS) * LO], fp16)
        raw = h.agg[:].bitcast(int32)
        src_in = [raw[:, k * KC:(k + 1) * KC] for k in range(2)]
        dst_in = [raw[:, (2 + k) * KC:(3 + k) * KC] for k in range(2)]
        hg = raw[:, 4 * KC:5 * KC]
        dcol = raw[:, 5 * KC:5 * KC + TILES]
        assert 5 * KC + TILES <= NP
        onehot_space = h.key1[:].bitcast(fp16)
        oh_hi = onehot_space[0:SR, 0:SAMP * W].rearrange("p (t n) -> p t n", n=W)
        oh_lo = onehot_space[0:SR, SAMP * W:SAMP * (W + P)].rearrange("p (t n) -> p t n", n=P)
        psy = [m.ps(f"psy{k}") for k in range(4)]
        psh, psp = m.ps("psh"), m.ps("psp")
        xt_in, keys_in = m.sems("xt_in", 2), m.sems("keys_in", 2)
        samples_in, dst_col_in, w_in, kept_in = m.sem("samples_in"), m.sem("dst_col_in"), m.sem("w_in"), m.sem("kept_in")
        iotas, masks = m.sem("iotas"), m.sem("masks")
        y_ready, y_out, y_stored = m.sem("y_ready"), m.sem("y_out"), m.sems("y_stored", 2)
        hg_ready, key1_ready, lo_ready, key2_ready = m.sem("hg_ready"), m.sem("key1_ready"), m.sem("lo_ready"), m.sem("key2_ready")
        split, onehots, counted = m.sem("split"), m.sem("onehots"), m.sem("counted")
        scan, prev_ready, first_ready, first_stored = m.sem("scan"), m.sem("prev_ready"), m.sem("first_ready"), m.sem("first_stored")
        seg, zeroed, pad_stored, cleared = m.sem("seg"), m.sem("zeroed"), m.sem("pad_stored"), m.sem("cleared")

        block = ctx.enter_context(nc.Block())

        @block.sync
        def _(sp):
            sp.dma_start(w1a[:], h.w1aT).then_inc(w_in, 16)
            sp.dma_start(b1b[:], h.b1.partition_broadcast(P)).then_inc(w_in, 16)
            for k in range(NC):
                if k >= 2:
                    sp.wait_ge(y_ready, 2 * (k - 1))
                sp.dma_start(xt[k % 2][:], h.xT[:, k * TC:(k + 1) * TC]).then_inc(xt_in[k % 2], 16)
                if k >= 1:
                    sp.wait_ge(y_out, 2 * k)
                    sp.dma_start(h.y_rows[k - 1], ysb[(k - 1) % 2][:]).then_inc(y_stored[(k - 1) % 2], 16)
            sp.wait_ge(y_out, 2 * NC)
            sp.dma_start(h.y_rows[NC - 1], ysb[(NC - 1) % 2][:]).then_inc(y_stored[(NC - 1) % 2], 16)
            for kept, given in h.weights:
                sp.dma_start(kept, given).then_inc(kept_in, 16)
            sp.wait_ge(kept_in, 16 * len(h.weights))
            sp.wait_ge(y_stored[0], 16 * ((NC + 1) // 2))
            sp.wait_ge(y_stored[1], 16 * (NC // 2))

        @block.scalar
        def _(act):
            act.dma_start(samp[:], h.samples).then_inc(samples_in, 16)
            act.dma_start(dcol, h.dst_col).then_inc(dst_col_in, 16)
            act.dma_start(dbase[:], h.dst_first.partition_broadcast(P)).then_inc(dst_col_in, 16)
            for k in range(KP):
                if k >= 2:
                    act.wait_ge(key1_ready, k - 1)
                    act.wait_ge(key2_ready, k - 1)
                act.dma_start(src_in[k % 2], h.src_keys[:, k * KC:(k + 1) * KC]).then_inc(keys_in[k % 2], 16)
                act.dma_start(dst_in[k % 2], h.dst_keys[:, k * KC:(k + 1) * KC]).then_inc(keys_in[k % 2], 16)
                if k >= 1:
                    act.wait_ge(lo_ready, k)
                    nc.scalar.copy(h.key2[:, (k - 1) * KC:k * KC], src_in[(k - 1) % 2]).then_inc(key2_ready, 1)
            act.wait_ge(lo_ready, KP)
            nc.scalar.copy(h.key2[:, (KP - 1) * KC:], src_in[(KP - 1) % 2]).then_inc(key2_ready, 1)
            act.wait_ge(zeroed, 1)
            for k in range(2):
                act.dma_start(h.A[k][:, GROUPS * LO:], zero[0:P // 2, :]).then_inc(pad_stored, 16)
            act.wait_ge(first_ready, 1)
            act.dma_start(h.first_of, first[:]).then_inc(first_stored, 16)
            act.wait_ge(first_stored, 16)
            act.wait_ge(pad_stored, 32)

        @block.gpsimd
        def _(pool):
            def iota(out, pattern):
                return nc.gpsimd.iota(out, pattern=pattern, base=0, channel_multiplier=0,
                                      allow_small_or_imprecise_dtypes=True)

            iota(h.iota_lo[:], [[1, LO]]).then_inc(iotas, 1)
            iota(h.iota_key[:], [[1, CH], [CH, GN]]).then_inc(iotas, 1)
            nc.gpsimd.memset(h.ones[:], 1.0).then_inc(masks, 1)
            nc.gpsimd.memset(h.ident[:], 0.0).then_inc(masks, 1)
            nc.gpsimd.memset(upper[:], 1.0).then_inc(masks, 1)
            nc.gpsimd.memset(zrow[:], 0.0).then_inc(masks, 1)
            nc.gpsimd.memset(h.ones16[:], 1.0).then_inc(masks, 1)
            nc.gpsimd.memset(h.rowsum[:, GROUPS:], 0.0).then_inc(masks, 1)
            pool.wait_ge(masks, 6)
            nc.gpsimd.affine_select(out=h.ident[:], in_=h.ident[:], compare_op=ALU.not_equal, fill=1.0, base=0,
                                    pattern=[[-1, P]], channel_multiplier=1).then_inc(masks, 1)
            nc.gpsimd.affine_select(out=upper[:], in_=upper[:], compare_op=ALU.is_gt, fill=0.0, base=0,
                                    pattern=[[1, W]], channel_multiplier=-1).then_inc(masks, 1)
            nc.gpsimd.memset(zero[:], 0.0).then_inc(zeroed, 1)
            pool.wait_ge(key1_ready, KP)
            pool.wait_ge(key2_ready, KP)
            pool.wait_ge(seg, 1)
            nc.gpsimd.memset(h.agg[:], 0.0).then_inc(cleared, 1)
            pool.wait_ge(cleared, 1)

        @block.vector
        def _(dve):
            V = nc.vector

            def sample_onehots():
                dve.wait_ge(samples_in, 16)
                V.tensor_single_scalar(s_hi[:], samp[:], 7, ALU.arith_shift_right).then_inc(split, 1)
                V.tensor_single_scalar(s_lo[:], samp[:], P - 1, ALU.bitwise_and).then_inc(split, 1)
                dve.wait_ge(split, 2)
                V.tensor_copy(f_hi[:], s_hi[:]).then_inc(split, 1)
                V.tensor_copy(f_lo[:], s_lo[:]).then_inc(split, 1)
                dve.wait_ge(iotas, 1)
                dve.wait_ge(split, 4)
                V.tensor_tensor(oh_hi, wide(f_hi[:], W), tall(h.iota_lo[0:SR, 0:W], SAMP),
                                ALU.is_equal).then_inc(onehots, 1)
                V.tensor_tensor(oh_lo, wide(f_lo[:], P), tall(h.iota_lo[0:SR, 0:P], SAMP),
                                ALU.is_equal).then_inc(onehots, 1)

            def segment_keys():
                dve.wait_ge(dst_col_in, 32)
                V.tensor_tensor(h.seg_key[:].rearrange("p (b t) -> p b t", t=BT),
                                dcol.rearrange("p (b t) -> p b t", t=BT), wide(dbase[:], BT),
                                ALU.subtract).then_inc(seg, 1)
                dve.wait_ge(seg, 1)
                V.tensor_scalar(inside[:], h.seg_key[:], 0.0, None, ALU.is_ge).then_inc(seg, 1)
                dve.wait_ge(seg, 2)
                V.scalar_tensor_tensor(held[:], h.seg_key[:], float(SEGW), inside[:], ALU.is_lt, ALU.mult,
                                       accum_out=h.caught[:, 0:1]).then_inc(seg, 1)

            def first_windows():
                dve.wait_ge(counted, 1)
                V.tensor_copy(hist[:], psh[0:W, 0:P]).then_inc(scan, 1)
                dve.wait_ge(masks, 6)
                dve.wait_ge(scan, 1)
                V.tensor_tensor_scan(cum[:], hist[:], zrow[:], 0.0, ALU.add, ALU.add).then_inc(scan, 1)
                dve.wait_ge(scan, 2)
                V.tensor_tensor(before[:], cum[:], hist[:], ALU.subtract).then_inc(scan, 1)
                dve.wait_ge(prev_ready, 1)
                V.tensor_copy(prev[:], psp[0:W, 0:1]).then_inc(scan, 1)
                dve.wait_ge(scan, 4)
                V.tensor_scalar(less[:], before[:], prev[:, 0:1], -1.0, ALU.add, ALU.add).then_inc(scan, 1)
                dve.wait_ge(scan, 5)
                V.tensor_scalar(first[:], less[:, ::GN], 0.0, None, ALU.max).then_inc(first_ready, 1)

            def keys(k):
                dve.wait_ge(keys_in[k % 2], 32 * (k // 2 + 1))
                reach(dve, key1_ready, k)
                if k == 0:
                    dve.wait_ge(counted, 1)
                V.tensor_single_scalar(hg, src_in[k % 2], CH - 1, ALU.bitwise_and).then_inc(hg_ready, 1)
                dve.wait_ge(hg_ready, k + 1)
                V.scalar_tensor_tensor(h.key1[:, k * KC:(k + 1) * KC], dst_in[k % 2], float(CH), hg,
                                       ALU.mult, ALU.add).then_inc(key1_ready, 1)
                V.tensor_single_scalar(src_in[k % 2], src_in[k % 2], 5, ALU.arith_shift_right).then_inc(lo_ready, 1)

            def y_copy(k):
                if k >= 2:
                    dve.wait_ge(y_stored[k % 2], 16 * (k // 2))
                for n, (lo, hi) in enumerate(halves_of):
                    dve.wait_ge(y_ready, 2 * k + n + 1)
                    V.tensor_tensor(ysb[k % 2][:, lo:hi, :],
                                    psy[(2 * k + n) % 4][:, 0:(hi - lo) * D].rearrange("p (j d) -> p j d", d=D),
                                    tall(b1b[:], hi - lo), ALU.add).then_inc(y_out, 1)

            sample_onehots()
            dve.wait_ge(w_in, 32)
            for k in range(NC):
                y_copy(k)
                if k == 2:
                    segment_keys()
                if k == 3:
                    first_windows()
                if 4 <= k < 4 + KP:
                    keys(k - 4)
            dve.wait_ge(seg, 3)

        @block.tensor
        def _(pe):
            pe.wait_ge(w_in, 32)
            for k in range(NC):
                pe.wait_ge(xt_in[k % 2], 16 * (k // 2 + 1))
                for n, (lo, hi) in enumerate(halves_of):
                    reach(pe, y_out, 2 * k + n - 3)
                    for j in range(lo, hi):
                        last = nc.tensor.matmul(psy[(2 * k + n) % 4][:, (j - lo) * D:(j - lo + 1) * D],
                                                xt[k % 2][:, j::NT], w1a[:], start=True, stop=True)
                    last.then_inc(y_ready, 1)
                if k == 1:
                    pe.wait_ge(onehots, 2)
                    for t in range(SAMP):
                        last = nc.tensor.matmul(psh[0:W, 0:P], oh_hi[:, t, :], oh_lo[:, t, :],
                                                start=(t == 0), stop=(t == SAMP - 1))
                    last.then_inc(counted, 1)
                if k == 3:
                    pe.wait_ge(masks, 8)
                    pe.wait_ge(scan, 2)
                    nc.tensor.matmul(psp[0:W, 0:1], upper[:], cum[:, P - 1:P], start=True,
                                     stop=True).then_inc(prev_ready, 1)


def edges(nc, h):
    with ExitStack() as ctx:
        m = Place(nc, ctx, "edges")
        idx = [m.sb(f"idx{k}", [P, BT], int32) for k in range(4)]
        places = m.sb("places", [1, (GPB + 1) * UN], int32)
        ea = [m.sb(f"ea{k}", [P, BE]) for k in range(2)]
        yg = [m.sb(f"yg{k}", [P, BT, D]) for k in range(4)]
        blk_key = [m.sb(f"blk_key{k}", [P, P]) for k in range(2)]
        hid = [m.sb(f"hid{k}", [P, BT, D]) for k in range(2)]
        seg1 = [m.sb(f"seg1{k}", [P, BT, SEGW]) for k in range(2)]
        row1 = [m.sb(f"row1{k}", [P, KT, P], fp16) for k in range(GPB)]
        col1 = [m.sb(f"col1{k}", [P, KT, LO], fp16) for k in range(GPB)]
        a_sb = [m.sb(f"a_sb{k}", [P, GPB, LO], fp16) for k in range(2)]
        pse = [m.ps(f"pse{k}", 1024) for k in range(2)]
        psa = [m.ps(f"psa{k}") for k in range(2)]
        pss = [m.ps(f"pss{k}") for k in range(2)]
        idx_in, places_in, places_read = m.sems("idx_in", 4), m.sem("places_in"), m.sem("places_read")
        ea_in, gathered, a_stored = m.sems("ea_in", 2), m.sems("gathered", 4), m.sems("a_stored", 2)
        e_done, sum_done, relu_done = m.sem("e_done"), m.sem("sum_done"), m.sem("relu_done")
        seg1_ready, seg_done, agg_done = m.sem("seg1_ready"), m.sem("seg_done"), m.sem("agg_done")
        hot_ready, a_done, a_out = m.sem("hot_ready"), m.sem("a_done"), m.sem("a_out")
        blk_key_ready, ea_zeroed, own_step = m.sem("blk_key_ready"), m.sem("ea_zeroed"), m.sem("own_step")

        block = ctx.enter_context(nc.Block())

        @block.sync
        def _(sp):
            def body(s):
                if s.c >= 4:
                    sp.wait_ge(gathered[s.c % 4], s.turn(4, 16 * BT, 1))
                sp.dma_start(idx[s.c % 4][:], h.src_idx[bass.ds(s.times(1), 1)]).then_inc(idx_in[s.c % 4], 16)
                reach(sp, e_done, s.times(1, -1))
                sp.dma_start(ea[s.c % 2][0:DE], h.ea_blocks[bass.ds(s.times(1), 1)]).then_inc(ea_in[s.c % 2], 16)

            def places_of(s, n, turn):
                reach(sp, places_read, turn)
                sp.dma_start(places[:, 0:GPB * n], h.first_group[:, bass.ds(s.times(GPB), GPB * n)]
                             ).then_inc(places_in, 16)
                late = 0 if s.c < LATE else LATE
                sp.dma_start(places[:, GPB * UN:GPB * UN + n], h.dst_first[:, bass.ds(s.times(1, -late), n)]
                             ).then_inc(places_in, 16)

            edge_loop(sp, body, places_of)
            reach(sp, places_read, PEEL + ROUNDS)
            sp.dma_start(places[:, 0:LATE], h.dst_first[:, BLOCKS - LATE:BLOCKS]).then_inc(places_in, 16)

        @block.gpsimd
        def _(pool):
            def body(s):
                pool.wait_ge(idx_in[s.c % 4], s.turn(4, 16))
                reach(pool, sum_done, s.times(1, -3))
                pool.sem_inc(own_step, 1)
                for t in range(BT):
                    nc.gpsimd.indirect_dma_start(
                        out=yg[s.c % 4][:, t, :], out_offset=None, in_=h.y,
                        in_offset=bass.IndirectOffsetOnAxis(ap=idx[s.c % 4][:, t:t + 1], axis=0)
                    ).then_inc(gathered[s.c % 4], 16)

            edge_loop(pool, body)

        @block.scalar
        def _(act):
            def store_a(s):
                act.wait_ge(a_out, s.times(GPB, GPB))
                for k in range(2):
                    act.dma_start(h.A[k][:, bass.ds(s.times(GPB * LO), GPB * LO)],
                                  a_sb[s.c % 2][k * P // 2:(k + 1) * P // 2].rearrange("p g l -> p (g l)")
                                  ).then_inc(a_stored[s.c % 2], 16)

            def body(s):
                if s.c >= 1:
                    store_a(s.back(1))
                if s.c >= 2:
                    act.wait_ge(a_stored[s.c % 2], s.turn(2, 32, 1))
                for j in range(GPB):
                    act.wait_ge(a_done, s.times(GPB, j + 1))
                    with nc.allow_low_precision("whole numbers up to 256"):
                        nc.scalar.activation(a_sb[s.c % 2][:, j, :], psa[(s.c + j) % 2][:, 0:LO], ACT.Copy,
                                             accum_out=h.rowsum[:, bass.ds(s.times(GPB, j), 1)]).then_inc(a_out, 1)
                act.wait_ge(sum_done, s.times(1, 1))
                reach(act, seg_done, s.times(1, -1))
                nc.scalar.activation(hid[s.c % 2][:], pse[s.c % 2][:, 0:BE].rearrange("p (t d) -> p t d", d=D),
                                     ACT.Relu).then_inc(relu_done, 1)

            edge_loop(act, body)
            store_a(Step(0, BLOCKS - 1))
            act.wait_ge(a_stored[0], 32 * ((BLOCKS + 1) // 2))
            act.wait_ge(a_stored[1], 32 * (BLOCKS // 2))

        @block.vector
        def _(dve):
            V = nc.vector

            regs = [dve.alloc_register(f"place{k}") for k in range((GPB + 1) * UN)]
            group_at, seg_at = [], []

            def read_places(s, n, turn):
                dve.wait_ge(places_in, turn * 32 + 32)
                dve.sem_inc(own_step, 1)
                dve.load(regs[0:GPB * n], places[0:1, 0:GPB * n])
                dve.load(regs[GPB * UN:GPB * UN + n], places[0:1, GPB * UN:GPB * UN + n]).then_inc(places_read, 1)
                group_at[:] = [dve.snap(r, min_val=0, max_val=KW - 1) for r in regs[0:GPB * n]]
                seg_at[:] = [dve.snap(r, min_val=0, max_val=NODES - 1) for r in regs[GPB * UN:GPB * UN + n]]

            def add_segment(s, at):
                dve.wait_ge(seg_done, s.times(1, 1))
                reach(dve, agg_done, s.times(1))
                V.tensor_tensor(h.agg[:, bass.ds(at, SEGW)], h.agg[:, bass.ds(at, SEGW)],
                                pss[s.c % 2][:, 0:SEGW], ALU.add).then_inc(agg_done, 1)

            def body(s):
                k = (s.c - PEEL) % UN if s.c >= PEEL else 0
                if s.c >= 1:
                    reach(dve, blk_key_ready, s.times(1))
                    V.tensor_scalar(blk_key[s.c % 2][:], blk_key[(s.c - 1) % 2][:], float(GPB * P), None,
                                    ALU.add).then_inc(blk_key_ready, 1)
                if s.c >= LATE:
                    add_segment(s.back(LATE), seg_at[k])
                dve.wait_ge(blk_key_ready, s.times(1, 1))
                for j in range(GPB):
                    u = group_at[GPB * k + j]
                    reach(dve, a_done, s.times(GPB, j + 1 - GPB))
                    V.scalar_tensor_tensor(row1[j][:], wide(h.key1[:, bass.DynSlice(u, KT, KS)], P), float(-P * j),
                                           tall(blk_key[s.c % 2][:], KT), ALU.add, ALU.is_equal)
                    for t in range(KT):
                        last = V.tensor_scalar(col1[j][:, t, :], h.iota_lo[:], h.key2[:, bass.ds(u + KS * t, 1)],
                                               None, ALU.is_equal)
                    last.then_inc(hot_ready, 1)
                reach(dve, seg_done, s.times(1, -1))
                V.tensor_tensor(seg1[s.c % 2][:], wide(h.seg_key[:, bass.ds(s.times(BT), BT)], SEGW),
                                tall(h.iota_lo[:, 0:SEGW], BT), ALU.is_equal).then_inc(seg1_ready, 1)

            V.tensor_copy(blk_key[0][:], h.iota_key[:]).then_inc(blk_key_ready, 1)
            for k in range(2):
                V.memset(ea[k][DE:P], 0.0).then_inc(ea_zeroed, 1)
            V.memset(h.w1b[DE:P], 0.0).then_inc(ea_zeroed, 1)
            edge_loop(dve, body, read_places)
            dve.wait_ge(places_in, 32 * (PEEL + ROUNDS) + 16)
            dve.load(regs[0:LATE], places[0:1, 0:LATE])
            for k in range(LATE):
                add_segment(Step(0, BLOCKS - LATE + k), dve.snap(regs[k], min_val=0, max_val=NODES - 1))

        @block.tensor
        def _(pe):
            def segment(s):
                pe.wait_ge(relu_done, s.times(1, 1))
                pe.wait_ge(seg1_ready, s.times(1, 1))
                reach(pe, agg_done, s.times(1, -1))
                for t in range(BT):
                    last = nc.tensor.matmul(pss[s.c % 2][:, 0:SEGW], hid[s.c % 2][:, t, :], seg1[s.c % 2][:, t, :],
                                            start=(t == 0), stop=(t == BT - 1))
                last.then_inc(seg_done, 1)

            def body(s):
                pe.wait_ge(ea_in[s.c % 2], s.turn(2, 16))
                reach(pe, relu_done, s.times(1, -1))
                for t in range(BT):
                    last = nc.tensor.matmul(pse[s.c % 2][:, t * D:(t + 1) * D], ea[s.c % 2][:, t * P:(t + 1) * P],
                                            h.w1b[:], start=(t % 4 == 0), stop=False)
                last.then_inc(e_done, 1)
                for j in range(GPB):
                    pe.wait_ge(hot_ready, s.times(GPB, j + 1))
                    reach(pe, a_out, s.times(GPB, j - 1))
                    for t in range(KT):
                        last = nc.tensor.matmul(psa[(s.c + j) % 2][:, 0:LO], row1[j][:, t, :], col1[j][:, t, :],
                                                start=(t == 0), stop=(t == KT - 1))
                    last.then_inc(a_done, 1)
                    if j == 1 and s.c >= 1:
                        segment(s.back(1))
                pe.wait_ge(gathered[s.c % 4], s.turn(4, 16 * BT))
                for lo in range(0, BT, 4):
                    hi = min(lo + 4, BT)
                    last = nc.tensor.matmul(pse[s.c % 2][:, lo * D:hi * D], h.ident[:], yg[s.c % 4][:, lo:hi, :],
                                            start=False, stop=True)
                last.then_inc(sum_done, 1)

            pe.wait_ge(ea_zeroed, 3)
            edge_loop(pe, body)
            segment(Step(0, BLOCKS - 1))


def verdict(nc, h):
    GC = GP // 7
    with ExitStack() as ctx:
        m = Place(nc, ctx, "verdict")
        rows, both = m.sb("rows", [P, 1]), m.sb("both", [P, 1])
        pick, pick16 = m.sb("pick", [P, GN]), m.sb("pick16", [P, GN], fp16)
        dd = m.sb("dd", [GN, GP])
        right = m.sb("right", [1, 1])
        w2, b2 = m.sb("w2", [D, D]), m.sb("b2", [D, 1])
        bih, bhh, bsum = m.sb("bih", [1, 3 * D]), m.sb("bhh", [1, 3 * D]), m.sb("bsum", [1, 4 * D])
        psd = [m.ps(f"psd{k}") for k in range(4)]
        pst, psw, psb = m.ps("pst"), m.ps("psw"), m.ps("psb")
        given, picked, total, told = m.sem("given"), m.sem("picked"), m.sem("total"), m.sem("told")
        deg_ready, deg_out, deg_stored = m.sem("deg_ready"), m.sem("deg_out"), m.sem("deg_stored")
        made, kept, sums, moved = m.sem("made"), m.sem("kept"), m.sem("sums"), m.sem("moved")

        block = ctx.enter_context(nc.Block())

        @block.sync
        def _(sp):
            for tile, data in ((w2[:], h.w2), (b2[:], h.b2), (bih[:], h.bih), (bhh[:], h.bhh)):
                sp.dma_start(tile, data).then_inc(given, 16)
            sp.wait_ge(deg_out, 7)
            sp.dma_start(h.deg.rearrange("a (d g) -> (a d) g", d=GN), dd[:]).then_inc(deg_stored, 16)
            sp.wait_ge(sums, 3)
            sp.dma_start(h.bias2[1:2, :], bsum[:]).then_inc(moved, 16)
            sp.wait_ge(deg_stored, 16)
            sp.wait_ge(moved, 16)

        @block.vector
        def _(dve):
            V = nc.vector
            V.tensor_reduce(rows[:], h.rowsum[:], AX.X, ALU.add).then_inc(picked, 1)
            V.tensor_reduce(pick[:], h.ident[:].rearrange("p (h d) -> p d h", d=GN), AX.X, ALU.add).then_inc(picked, 1)
            dve.wait_ge(picked, 2)
            V.tensor_tensor(both[:], rows[:], h.caught[:], ALU.add).then_inc(picked, 1)
            V.tensor_copy(pick16[:], pick[:]).then_inc(picked, 1)
            dve.wait_ge(total, 1)
            V.tensor_scalar(right[:], pst[0:1, 0:1], float(2 * EDGES), None, ALU.is_equal).then_inc(told, 1)
            dve.wait_ge(told, 1)
            V.tensor_copy(h.sorted[:], right[:]).then_inc(told, 1)
            for k in range(7):
                dve.wait_ge(deg_ready, k + 1)
                V.tensor_copy(dd[:, k * GC:(k + 1) * GC], psd[k % 4][0:GN, 0:GC]).then_inc(deg_out, 1)
            dve.wait_ge(made, 2)
            V.tensor_copy(h.wc[:], psw[:, 0:3 * D]).then_inc(kept, 1)
            V.memset(h.bias2[0:1, 3 * D:], 0.0).then_inc(kept, 1)
            V.tensor_copy(h.bias2[0:1, 0:3 * D], psb[0:1, 0:3 * D]).then_inc(kept, 1)
            dve.wait_ge(given, 64)
            V.tensor_copy(bsum[:, 0:D], bih[:, 0:D]).then_inc(sums, 1)
            V.tensor_tensor(bsum[:, D:3 * D], bih[:, D:3 * D], bhh[:, 0:2 * D], ALU.add).then_inc(sums, 1)
            V.tensor_copy(bsum[:, 3 * D:], bhh[:, 2 * D:]).then_inc(sums, 1)

        @block.tensor
        def _(pe):
            pe.wait_ge(picked, 4)
            nc.tensor.matmul(pst[0:1, 0:1], both[:], h.ones[:, 0:1], start=True, stop=True).then_inc(total, 1)
            for k in range(7):
                reach(pe, deg_out, k - 3)
                nc.tensor.matmul(psd[k % 4][0:GN, 0:GC], pick16[:], h.rowsum[:, k * GC:(k + 1) * GC],
                                 start=True, stop=True).then_inc(deg_ready, 1)
            pe.wait_ge(given, 64)
            nc.tensor.matmul(psw[:, 0:3 * D], w2[:], h.wih[:], start=True, stop=True).then_inc(made, 1)
            nc.tensor.matmul(psb[0:1, 0:3 * D], b2[:], h.wih[:], start=True, stop=True).then_inc(made, 1)


def general(nc, h, layer):
    with ExitStack() as ctx:
        m = Place(nc, ctx, f"general{layer}")
        dsum = m.sb("dsum", [P, NP])
        row = m.sb("row", [1, NP] if layer == 0 else [1, 1])
        idx, to = m.sb("idx", [P, BT], int32), m.sb("to", [P, BT], int32)
        ea = m.sb("ea", [P, BE])
        got, hid = m.sb("got", [P, BT, D]), m.sb("hid", [P, BT, D])
        key = [m.sb(f"key{k}", [P, BT]) for k in range(2)]
        hot = m.sb("hot", [P, BT, LO])
        mt = m.sb("mt", [P, LO])
        inv = m.sb("inv", [P, LO])
        pse = m.ps("pse", 1024)
        psf, psg = m.ps("psf"), m.ps("psg")
        loaded, gathered = m.sem("loaded"), m.sem("gathered")
        e_done, hid_ready, blocks_done = m.sem("e_done"), m.sem("hid_ready"), m.sem("blocks_done")
        key_ready, hot_ready, summed, added = m.sem("key_ready"), m.sem("hot_ready"), m.sem("summed"), m.sem("added")
        cleared, deg_row, deg_stored = m.sem("cleared"), m.sem("deg_row"), m.sem("deg_stored")
        own_step = m.sem("general_step")
        fin = finish_buffers(m) if layer else None

        def unsorted(eng):
            return eng.If(1 - eng.value_load(h.sorted[0:1, 0:1], min_val=0, max_val=1))

        block = ctx.enter_context(nc.Block())

        @block.sync
        def _(sp):
            with unsorted(sp):
                with sp.Fori(0, BLOCKS) as b:
                    sp.wait_ge(blocks_done, b + 1)
                    sp.dma_start(idx[:], (h.dst_idx if layer else h.src_idx)[bass.ds(b, 1)]).then_inc(loaded, 16)
                    sp.dma_start(to[:], (h.src_idx if layer else h.dst_idx)[bass.ds(b, 1)]).then_inc(loaded, 16)
                    if layer == 0:
                        sp.dma_start(ea[0:DE], h.ea_blocks[bass.ds(b, 1)]).then_inc(loaded, 16)
                if layer == 0:
                    sp.wait_ge(deg_row, 1)
                    sp.dma_start(h.deg, row[:]).then_inc(deg_stored, 16)
                    sp.wait_ge(deg_stored, 16)
                else:
                    finish_sync(nc, sp, h, fin)

        @block.gpsimd
        def _(pool):
            with unsorted(pool):
                with pool.Fori(0, BLOCKS) as b:
                    pool.wait_ge(loaded, (b + 1) * (32 if layer else 48))
                    pool.sem_inc(own_step, 1)
                    for t in range(BT):
                        nc.gpsimd.indirect_dma_start(
                            out=got[:, t, :], out_offset=None, in_=h.x1 if layer else h.y,
                            in_offset=bass.IndirectOffsetOnAxis(ap=idx[:, t:t + 1], axis=0)).then_inc(gathered, 16)

        @block.scalar
        def _(act):
            with unsorted(act):
                with act.Fori(0, BLOCKS) as b:
                    act.wait_ge(e_done, b + 1) if layer == 0 else act.wait_ge(gathered, (b + 1) * (16 * BT))
                    nc.scalar.activation(hid[:], pse[:, 0:BE].rearrange("p (t d) -> p t d", d=D) if layer == 0
                                         else got[:], ACT.Copy if layer else ACT.Relu).then_inc(hid_ready, 1)
                if layer:
                    finish_scalar(nc, act, h, fin)

        @block.vector
        def _(dve):
            V = nc.vector
            with unsorted(dve):
                V.memset(h.agg[:], 0.0).then_inc(cleared, 1)
                V.memset(dsum[:], 0.0).then_inc(cleared, 1)
                if layer == 0:
                    V.memset(ea[DE:P], 0.0).then_inc(cleared, 1)
                dve.wait_ge(cleared, 2)
                dve.sem_inc(blocks_done, 1)
                with dve.Fori(0, BLOCKS) as b:
                    dve.wait_ge(loaded, (b + 1) * (32 if layer else 48))
                    V.tensor_copy(key[0][:], to[:]).then_inc(key_ready, 1)
                    dve.wait_ge(hid_ready, b + 1)
                    dve.sem_inc(own_step, 1)
                    with dve.Fori(0, CH // 2) as pair:
                        for k in range(2):
                            dve.wait_ge(key_ready, b * (CH + 1) + pair * 2 + (k + 1))
                            V.tensor_tensor(hot[:], wide(key[k][:], LO), tall(h.iota_lo[:], BT),
                                            ALU.is_equal).then_inc(hot_ready, 1)
                            V.tensor_scalar(key[1 - k][:], key[k][:], -float(LO), None,
                                            ALU.add).then_inc(key_ready, 1)
                            dve.wait_ge(summed, b * CH + pair * 2 + (k + 1))
                            at = bass.ds(pair * (2 * LO) + k * LO, LO)
                            V.tensor_tensor(h.agg[:, at], h.agg[:, at], psf[:, 0:LO], ALU.add).then_inc(added, 1)
                            V.tensor_tensor(dsum[:, at], dsum[:, at], psg[:, 0:LO], ALU.add).then_inc(added, 1)
                            dve.wait_ge(added, b * (2 * CH) + pair * 4 + (2 * k + 2))
                    dve.sem_inc(blocks_done, 1)
                if layer == 0:
                    V.tensor_copy(row[:].rearrange("a (d g) -> a g d", d=GN),
                                  dsum[0:1, :].rearrange("a (g d) -> a g d", d=GN)).then_inc(deg_row, 1)
                else:
                    finish_vector(nc, dve, h, fin,
                                  lambda s: h.agg[:].rearrange("f (l c) -> f c l", c=CH)[:, bass.ds(s, 1), :],
                                  lambda s: dsum[:].rearrange("f (l c) -> f c l", c=CH)[:, bass.ds(s, 1), :], 1.0)

        @block.tensor
        def _(pe):
            with unsorted(pe):
                pe.wait_ge(cleared, 3 if layer == 0 else 2)
                with pe.Fori(0, BLOCKS) as b:
                    if layer == 0:
                        pe.wait_ge(loaded, (b + 1) * 48)
                        pe.wait_ge(gathered, (b + 1) * (16 * BT))
                        for t in range(BT):
                            nc.tensor.matmul(pse[:, t * D:(t + 1) * D], ea[:, t * P:(t + 1) * P], h.w1b[:],
                                             start=True, stop=False)
                            last = nc.tensor.matmul(pse[:, t * D:(t + 1) * D], h.ident[:], got[:, t, :],
                                                    start=False, stop=True)
                        last.then_inc(e_done, 1)
                    pe.wait_ge(hid_ready, b + 1)
                    pe.sem_inc(own_step, 1)
                    with pe.Fori(0, CH) as c:
                        pe.wait_ge(hot_ready, b * CH + c + 1)
                        for t in range(BT):
                            nc.tensor.matmul(psf[:, 0:LO], hid[:, t, :], hot[:, t, :], start=(t == 0),
                                             stop=(t == BT - 1))
                        for t in range(BT):
                            last = nc.tensor.matmul(psg[:, 0:LO], h.ones[:], hot[:, t, :], start=(t == 0),
                                                    stop=(t == BT - 1))
                        last.then_inc(summed, 1)
                if layer:
                    finish_tensor(nc, pe, h, fin)


def batch_loop(eng, body):
    for c in range(2):
        body(Step(0, c, 2))
    with eng.Fori(0, NB // 2 - 1) as i:
        for k in range(2):
            body(Step(i, 2 + k, 2))


def gates(nc, h):
    BC = WB * P
    with ExitStack() as ctx:
        m = Place(nc, ctx, "gates")
        xt = [m.sb(f"gxt{k}", [D, BC]) for k in range(2)]
        xq = [m.sb(f"gxq{k}", [P, WB, D]) for k in range(2)]
        deg2 = [m.sb(f"deg2{k}", [2, BC]) for k in range(2)]
        ag = [m.sb(f"ag{k}", [D, WB, P]) for k in range(2)]
        rz = [m.sb(f"rz{k}", [P, WB, 2 * D]) for k in range(2)]
        tt = [m.sb(f"tt{k}", [P, WB, D]) for k in range(2)]
        nn = [m.sb(f"nn{k}", [P, WB, D]) for k in range(2)]
        df = m.sb("df", [P, WB, D])
        vb = [m.sb(f"vb{k}", [P, WB, D]) for k in range(2)]
        st, mvb = m.sb("st", [P, WB, 6]), m.sb("mvb", [P, WB, 2])
        psn = [m.ps(f"psn{k}") for k in range(7)]
        xt_in, xq_in, deg_in = m.sems("gxt_in", 2), m.sems("gxq_in", 2), m.sems("deg_in", 2)
        ones_set, ag_ready, g_done, rz_ready = m.sem("ones_set"), m.sem("ag_ready"), m.sem("g_done"), m.sem("rz_ready")
        rh_done, t_ready, n_ready = m.sem("rh_done"), m.sem("t_ready"), m.sem("n_ready")
        mix, v_done, stats, v_kept, own_step = m.sem("mix"), m.sem("v_done"), m.sem("stats"), m.sem("v_kept"), m.sem("own_step")

        block = ctx.enter_context(nc.Block())

        @block.sync
        def _(sp):
            sp.wait_ge(ones_set, 2)

            def body(s):
                k = s.c % 2
                reach(sp, t_ready, s.times(WB, -WB))
                sp.dma_start(xt[k][:], h.xT_tiles[:, bass.ds(s.times(BC), BC)]).then_inc(xt_in[k], 16)
                sp.dma_start(deg2[k][0:1, :].rearrange("a (q w) -> a q w", w=WB),
                             h.deg.rearrange("a (q w) -> a q w", w=W)[:, :, bass.ds(s.times(WB), WB)]
                             ).then_inc(deg_in[k], 16)
                reach(sp, v_done, s.times(1, -1))
                sp.dma_start(xq[k][:], h.x_tiles[:, bass.ds(s.times(WB * D), WB * D)]).then_inc(xq_in[k], 16)

            batch_loop(sp, body)

        @block.gpsimd
        def _(pool):
            def body(s):
                pool.wait_ge(v_done, s.times(1, 1))
                nc.gpsimd.tensor_copy(h.v[:, bass.ds(s.times(WB), WB), :], vb[s.c % 2][:]).then_inc(v_kept, 1)

            batch_loop(pool, body)

        @block.scalar
        def _(act):
            agg = h.agg[:].rearrange("f (g w d) -> f w d g", w=W, d=GN)

            def body(s):
                k = s.c % 2
                reach(act, g_done, s.times(WB, -WB))
                nc.scalar.copy(ag[k][:].rearrange("f w (d g) -> f w d g", d=GN),
                               agg[:, bass.ds(s.times(WB), WB)]).then_inc(ag_ready, 1)
                reach(act, v_done, s.times(1, -1))
                for w in range(WB):
                    act.wait_ge(g_done, s.times(WB, w + 1))
                    nc.scalar.activation(rz[k][:, w, :], psn[w][:, D:3 * D], ACT.Sigmoid).then_inc(rz_ready, 1)
                act.wait_ge(t_ready, s.times(WB, WB))
                nc.scalar.activation(nn[k][:], tt[k][:], ACT.Tanh).then_inc(n_ready, 1)

            batch_loop(act, body)

        @block.vector
        def _(dve):
            V = nc.vector

            def blend(s):
                k = s.c % 2
                dve.wait_ge(n_ready, s.times(1, 1))
                dve.wait_ge(xq_in[k], s.turn(2, 16))
                reach(dve, stats, s.times(2 * WB + 1))
                V.tensor_tensor(df[:], xq[k][:], nn[k][:], ALU.subtract).then_inc(mix, 1)
                dve.wait_ge(mix, s.times(3, 1))
                V.tensor_tensor(df[:], df[:], rz[k][:, :, D:], ALU.mult).then_inc(mix, 1)
                V.tensor_tensor(nn[k][:], nn[k][:], xq[k][:], ALU.add).then_inc(mix, 1)
                dve.wait_ge(mix, s.times(3, 3))
                reach(dve, v_kept, s.times(1, -1))
                V.tensor_tensor(vb[k][:], df[:], nn[k][:], ALU.add).then_inc(v_done, 1)
                dve.wait_ge(v_done, s.times(1, 1))
                dve.sem_inc(own_step, 1)
                for w in range(WB):
                    V.bn_stats(st[:, w, :], vb[k][:, w, :]).then_inc(stats, 1)
                dve.wait_ge(stats, s.times(2 * WB + 1, WB))
                dve.sem_inc(own_step, 1)
                for w in range(WB):
                    V.bn_aggr(mvb[:, w, :], st[:, w, :]).then_inc(stats, 1)
                dve.wait_ge(stats, s.times(2 * WB + 1, 2 * WB))
                V.tensor_copy(h.mv[:, bass.ds(s.times(WB), WB), :], mvb[:]).then_inc(stats, 1)

            def body(s):
                k = s.c % 2

                def add_in(w):
                    dve.wait_ge(rh_done, s.times(WB, w + 1))
                    V.tensor_tensor(tt[k][:, w, :], tt[k][:, w, :], psn[w][:, 0:D], ALU.add).then_inc(t_ready, 1)

                reach(dve, n_ready, s.times(1, -1))
                for w in range(WB):
                    dve.wait_ge(rz_ready, s.times(WB, w + 1))
                    V.tensor_tensor(tt[k][:, w, :], rz[k][:, w, 0:D], psn[w][:, 3 * D:], ALU.mult).then_inc(rh_done, 1)
                    if w:
                        add_in(w - 1)
                add_in(WB - 1)
                if s.c >= 1:
                    blend(s.back(1))

            for k in range(2):
                V.memset(deg2[k][:], 1.0).then_inc(ones_set, 1)
            batch_loop(dve, body)
            blend(Step(0, NB - 1, 2))

        @block.tensor
        def _(pe):
            def body(s):
                k = s.c % 2
                pe.wait_ge(xt_in[k], s.turn(2, 16))
                pe.wait_ge(deg_in[k], s.turn(2, 16))
                pe.wait_ge(ag_ready, s.times(1, 1))
                for w in range(WB):
                    reach(pe, t_ready, s.times(WB, w + 1 - WB))
                    nc.tensor.matmul(psn[w][:], deg2[k][:, w::WB], h.bias2[:], start=True, stop=False)
                    nc.tensor.matmul(psn[w][:, 0:3 * D], ag[k][:, w, :], h.wc[:], start=False, stop=False)
                    nc.tensor.matmul(psn[w][:, D:], xt[k][:, w * P:(w + 1) * P], h.whh[:], start=False,
                                     stop=True).then_inc(g_done, 1)

            batch_loop(pe, body)


def normalise(nc, h):
    with ExitStack() as ctx:
        m = Place(nc, ctx, "normalise")
        var, std = m.sb("var", [P, W]), m.sb("std", [P, W])
        rstd = m.sb("rstd", [P, W])
        xb = [m.sb(f"xb{k}", [P, WB, D]) for k in range(2)]
        xtb = [m.sb(f"xtb{k}", [D, WB, P]) for k in range(2)]
        rb = [m.sb(f"rb{k}", [P, WB, D]) for k in range(2)]
        pst = [m.ps(f"pstr{k}", 1024) for k in range(2)]
        psr = [m.ps(f"psr{k}", 1024) for k in range(2)]
        moments, xb_ready, hi_ready, lo_ready = m.sem("moments"), m.sem("xb_ready"), m.sem("hi_ready"), m.sem("nlo_ready")
        turned, xtb_ready, r_done, rb_ready = m.sem("turned"), m.sem("xtb_ready"), m.sem("r_done"), m.sem("rb_ready")
        r_stored, x_stored = m.sems("r_stored", 2), m.sems("x_stored", 2)

        block = ctx.enter_context(nc.Block())

        @block.sync
        def _(sp):
            def body(s):
                k = s.c % 2
                sp.wait_ge(xb_ready, s.times(WB, WB))
                for d in range(GN):
                    sp.dma_start(h.x1.rearrange("(g w d) f -> d g w f", w=W, d=GN)[d, :, bass.ds(s.times(WB), WB), :],
                                 xb[k][d * GR:(d + 1) * GR]).then_inc(x_stored[k], 16)
                sp.wait_ge(rb_ready, s.times(1, 1))
                for d in range(GN):
                    sp.dma_start(h.r.rearrange("(g w d) f -> d g w f", w=W, d=GN)[d, :, bass.ds(s.times(WB), WB), :],
                                 rb[k][d * GR:(d + 1) * GR]).then_inc(r_stored[k], 16)

            batch_loop(sp, body)
            for k in range(2):
                sp.wait_ge(x_stored[k], 16 * GN * NB // 2)
                sp.wait_ge(r_stored[k], 16 * GN * NB // 2)

        @block.scalar
        def _(act):
            act.wait_ge(moments, 1)
            nc.scalar.activation(std[:], var[:], ACT.Sqrt).then_inc(moments, 1)

            def body(s):
                k = s.c % 2
                act.wait_ge(xb_ready, s.times(WB, WB))
                nc.scalar.activation(h.x1s[:, bass.ds(s.times(WB), WB), 0, :], xb[k][:], ACT.Copy,
                                     scale=SCALE).then_inc(hi_ready, 1)
                act.wait_ge(turned, s.times(1, 1))
                reach(act, r_done, s.times(1, -1))
                nc.scalar.copy(xtb[k][:], pst[k][:, 0:WB * P].rearrange("f (w p) -> f w p", p=P)).then_inc(xtb_ready, 1)

            batch_loop(act, body)

        @block.vector
        def _(dve):
            V = nc.vector
            V.tensor_scalar(var[:], h.mv[:, :, 1], EPS, None, ALU.add).then_inc(moments, 1)
            dve.wait_ge(moments, 2)
            V.reciprocal(rstd[:], std[:]).then_inc(moments, 1)
            dve.wait_ge(moments, 3)

            def second(s):
                k = s.c % 2
                dve.wait_ge(hi_ready, s.times(1, 1))
                V.scalar_tensor_tensor(h.x1s[:, bass.ds(s.times(WB), WB), 1, :], xb[k][:], SCALE,
                                       h.x1s[:, bass.ds(s.times(WB), WB), 0, :], ALU.mult,
                                       ALU.subtract).then_inc(lo_ready, 1)
                dve.wait_ge(r_done, s.times(1, 1))
                if s.c >= 2:
                    dve.wait_ge(r_stored[k], s.turn(2, 16 * GN, 1))
                V.tensor_tensor(rb[k][:], psr[k][:, 0:WB * D].rearrange("p (w d) -> p w d", d=D), xb[k][:],
                                ALU.add).then_inc(rb_ready, 1)

            def body(s):
                k = s.c % 2
                if s.c >= 2:
                    dve.wait_ge(x_stored[k], s.turn(2, 16 * GN, 1))
                    dve.wait_ge(rb_ready, s.times(1, -1))
                    dve.wait_ge(lo_ready, s.times(1, -1))
                for w in range(WB):
                    one = bass.ds(s.times(WB, w), 1)
                    V.tensor_scalar(xb[k][:, w, :], h.v[:, one, :].rearrange("p a d -> p (a d)"),
                                    h.mv[:, one, 0], rstd[:, one], ALU.subtract, ALU.mult).then_inc(xb_ready, 1)
                if s.c >= 1:
                    second(s.back(1))

            batch_loop(dve, body)
            second(Step(0, NB - 1, 2))

        @block.tensor
        def _(pe):
            def root(s):
                k = s.c % 2
                pe.wait_ge(xtb_ready, s.times(1, 1))
                reach(pe, rb_ready, s.times(1, -1))
                for lo in range(0, WB, 4):
                    hi = min(lo + 4, WB)
                    nc.tensor.matmul(psr[k][:, lo * D:hi * D], h.ones[0:1, :], h.bias4[:, 0:(hi - lo) * D],
                                     start=True, stop=False)
                    for w in range(lo, hi):
                        last = nc.tensor.matmul(psr[k][:, w * D:(w + 1) * D], xtb[k][:, w, :], h.root[:],
                                                start=False, stop=(w == hi - 1))
                last.then_inc(r_done, 1)

            def body(s):
                k = s.c % 2
                reach(pe, xtb_ready, s.times(1, -1))
                for w in range(WB):
                    pe.wait_ge(xb_ready, s.times(WB, w + 1))
                    last = nc.tensor.transpose(pst[k][:, w * P:(w + 1) * P], xb[k][:, w, :], h.ident[:])
                last.then_inc(turned, 1)
                if s.c >= 1:
                    root(s.back(1))

            batch_loop(pe, body)
            root(Step(0, NB - 1, 2))


def finish_buffers(m):
    f = Shared()
    f.inv = [m.sb(f"inv{k}", [P, LO]) for k in range(2)]
    f.mean = [m.sb(f"mean{k}", [P, LO]) for k in range(2)]
    f.r = [m.sb(f"r_sb{k}", [SM, SJ, D]) for k in range(2)]
    f.o = [m.sb(f"o{k}", [SM, SJ, D]) for k in range(2)]
    f.out = [m.sb(f"out{k}", [SM, SJ, D]) for k in range(2)]
    f.st, f.mv = m.sb("fst", [SM, SJ, 6]), m.sb("fmv", [SM, SJ, 2])
    f.var, f.std, f.rstd = m.sb("fvar", [SM, SJ]), m.sb("fstd", [SM, SJ]), m.sb("frstd", [SM, SJ])
    f.ps = [m.ps(f"pso{k}") for k in range(2)]
    f.r_in, f.stored = m.sems("r_in", 2), m.sems("stored", 2)
    f.steps, f.mean_ready, f.product = m.sem("steps"), m.sem("mean_ready"), m.sem("product")
    f.norm, f.own_step = m.sem("norm"), m.sem("own_step")
    f.added, f.var_ready, f.std_ready, f.out_ready = m.sem("fadded"), m.sem("var_ready"), m.sem("std_ready"), m.sem("out_ready")
    return f


class Chunk(Step):

    def __init__(self, i, c):
        super().__init__(i, c, 2)

    def back(self, n):
        return Chunk(self.i, self.c - n)


def chunk_rows(t, s):
    return t.rearrange("(j p c) f -> c p j f", j=SJ, c=CH)[bass.ds(s.times(1), 1)]


def finish_loads(nc, sp, h, f, s):
    k = s.c % 2
    reach(sp, f.added, s.times(1, -1))
    sp.dma_start(f.r[k][:], chunk_rows(h.r, s)).then_inc(f.r_in[k], 16)


def finish_stores(nc, sp, h, f, s):
    k = s.c % 2
    sp.wait_ge(f.out_ready, s.times(SJ, SJ))
    sp.dma_start(chunk_rows(h.out, s), f.out[k][:]).then_inc(f.stored[k], 16)


def finish_product(nc, pe, h, f, s):
    k = s.c % 2
    pe.wait_ge(f.mean_ready, s.times(1, 1))
    reach(pe, f.added, s.times(1, -1))
    for j in range(SJ):
        last = nc.tensor.matmul(f.ps[k][0:SM, j * D:(j + 1) * D], f.mean[k][:, j * SM:(j + 1) * SM], h.weight[:],
                                start=True, stop=True)
    last.then_inc(f.product, 1)


def finish_root(nc, act, h, f, s):
    act.wait_ge(f.var_ready, s.times(1, 1))
    nc.scalar.activation(f.std[:], f.var[:], ACT.Sqrt).then_inc(f.std_ready, 1)


def finish_mean(nc, dve, h, f, s, sums, degs, scale):
    V = nc.vector
    k = s.c % 2
    reach(dve, f.product, s.times(1, -1))
    V.tensor_scalar(f.inv[k][:], degs, 1.0, None, ALU.max).then_inc(f.steps, 1)
    dve.wait_ge(f.steps, s.times(2, 1))
    V.reciprocal(f.inv[k][:], f.inv[k][:]).then_inc(f.steps, 1)
    dve.wait_ge(f.steps, s.times(2, 2))
    V.scalar_tensor_tensor(f.mean[k][:], sums, scale, f.inv[k][:], ALU.mult, ALU.mult).then_inc(f.mean_ready, 1)


def finish_norm(nc, dve, h, f, s):
    V = nc.vector
    k = s.c % 2
    dve.wait_ge(f.product, s.times(1, 1))
    dve.wait_ge(f.r_in[k], s.turn(2, 16))
    V.tensor_tensor(f.o[k][:], f.ps[k][0:SM, :].rearrange("p (j d) -> p j d", d=D), f.r[k][:],
                    ALU.add).then_inc(f.added, 1)
    dve.wait_ge(f.added, s.times(1, 1))
    reach(dve, f.out_ready, s.times(SJ))
    dve.sem_inc(f.own_step, 1)
    for j in range(SJ):
        V.bn_stats(f.st[:, j, :], f.o[k][:, j, :]).then_inc(f.norm, 1)
    dve.wait_ge(f.norm, s.times(2 * SJ + 1, SJ))
    dve.sem_inc(f.own_step, 1)
    for j in range(SJ):
        V.bn_aggr(f.mv[:, j, :], f.st[:, j, :]).then_inc(f.norm, 1)
    dve.wait_ge(f.norm, s.times(2 * SJ + 1, 2 * SJ))
    V.tensor_scalar(f.var[:], f.mv[:, :, 1], EPS, None, ALU.add).then_inc(f.var_ready, 1)
    dve.wait_ge(f.std_ready, s.times(1, 1))
    V.reciprocal(f.rstd[:], f.std[:]).then_inc(f.norm, 1)
    dve.wait_ge(f.norm, s.times(2 * SJ + 1, 2 * SJ + 1))
    reach_stored(dve, f, s)
    for j in range(SJ):
        V.tensor_scalar(f.out[k][:, j, :], f.o[k][:, j, :], f.mv[:, j, 0:1], f.rstd[:, j:j + 1],
                        ALU.subtract, ALU.mult).then_inc(f.out_ready, 1)


def reach_stored(dve, f, s):
    if s.c >= 2:
        dve.wait_ge(f.stored[s.c % 2], s.turn(2, 16, 1))


def chunk_loop(eng, body):
    for c in range(2):
        body(Chunk(0, c), 0)
    with eng.Fori(0, CH // 4 - 1) as i:
        for k in range(2):
            body(Chunk(i, 2 + k), 0)
    with eng.Fori(0, CH // 4) as i:
        for k in range(2):
            body(Chunk(i, CH // 2 + k), 1)


def finish_sync(nc, sp, h, f):
    def body(s, half):
        finish_loads(nc, sp, h, f, s)
        finish_stores(nc, sp, h, f, s)
    chunk_loop(sp, body)
    for k in range(2):
        sp.wait_ge(f.stored[k], 16 * CH // 2)


def finish_scalar(nc, act, h, f):
    chunk_loop(act, lambda s, half: finish_root(nc, act, h, f, s))


def finish_tensor(nc, pe, h, f):
    chunk_loop(pe, lambda s, half: finish_product(nc, pe, h, f, s))


def finish_vector(nc, dve, h, f, sums, degs, scale):
    def body(s, half):
        finish_mean(nc, dve, h, f, s, sums(s.times(1)), degs(s.times(1)), scale)
        finish_norm(nc, dve, h, f, s)
    chunk_loop(dve, body)


def sources(nc, h):
    AC = AW * LO
    with ExitStack() as ctx:
        m = Place(nc, ctx, "sources")
        a = [m.sb(f"a{k}", [P, AW, LO], fp16) for k in range(AL)]
        six = m.sb("six", [P, 6, LO], fp16)
        four, two = m.sb("four", [P, 4, LO], fp16), [m.sb(f"two{k}", [P, 2, LO], fp16) for k in range(2)]
        psx, psg = [m.ps(f"psx{k}") for k in range(2)], [m.ps(f"psg{k}") for k in range(2)]
        f = finish_buffers(m)
        a_in, own_step = m.sems("a_in", AL), m.sem("load_step")
        a_used, halved, fold, two_ready, deg_done = m.sem("a_used"), m.sem("halved"), m.sem("fold"), m.sem("two_ready"), m.sem("deg_done")

        def if_sorted(eng):
            return eng.If(eng.value_load(h.sorted[0:1, 0:1], min_val=0, max_val=1))

        block = ctx.enter_context(nc.Block())

        @block.sync
        def _(sp):
            def body(s, half):
                rows = h.A[half].rearrange("(c d) (g x) -> c (d g) x", d=GN, g=GR)
                for l in range(AL):
                    reach(sp, a_used, s.times(AL, l + 1 - AL))
                    sp.sem_inc(own_step, 1)
                    reach(sp, halved, s.times(2 * AL, 2 * (l + 1 - AL)))
                    sp.sem_inc(own_step, 1)
                    sp.dma_start(a[l][:].rearrange("p w l -> p (w l)"),
                                 rows[bass.ds(s.times(1, -half * CH // 2), 1), :, l * AC:(l + 1) * AC]
                                 ).then_inc(a_in[l], 16)
                    if l == 1:
                        finish_loads(nc, sp, h, f, s)
                    if l == AL - 2 and s.c >= 1:
                        finish_stores(nc, sp, h, f, s.back(1))

            with if_sorted(sp):
                chunk_loop(sp, body)
                finish_stores(nc, sp, h, f, Chunk(0, CH - 1))
                for k in range(2):
                    sp.wait_ge(f.stored[k], 16 * CH // 2)

        @block.scalar
        def _(act):
            with if_sorted(act):
                finish_scalar(nc, act, h, f)

        @block.vector
        def _(dve):
            V = nc.vector

            def fold_tiles(s, l):
                n = (s.c * AL + l) % 2
                at = s.times(AL, l)
                dve.wait_ge(a_in[l], s.times(16, 16))
                if not (isinstance(at, int) and at == 0):
                    dve.wait_ge(fold, at)
                    dve.wait_ge(two_ready, at)
                V.tensor_tensor(six[:], a[l][:, 0:6], a[l][:, 7:13], ALU.add).then_inc(halved, 1)
                V.tensor_tensor(four[:, 3], a[l][:, 6], a[l][:, 13], ALU.add).then_inc(halved, 1)
                dve.wait_ge(halved, s.times(2 * AL, 2 * l + 2))
                V.tensor_tensor(four[:, 0:3], six[:, 0:3], six[:, 3:6], ALU.add).then_inc(fold, 1)
                dve.wait_ge(fold, s.times(AL, l + 1))
                reach(dve, deg_done, s.times(AL, l - 1))
                V.tensor_tensor(two[n][:], four[:, 0:2], four[:, 2:4], ALU.add).then_inc(two_ready, 1)

            def body(s, half):
                for l in range(AL):
                    fold_tiles(s, l)
                    if l == 1 and s.c >= 1:
                        mean(s.back(1))
                    if l == 3 and s.c >= 1:
                        finish_norm(nc, dve, h, f, s.back(1))

            def mean(s):
                dve.wait_ge(a_used, s.times(AL, AL))
                dve.wait_ge(deg_done, s.times(AL, AL))
                finish_mean(nc, dve, h, f, s, psx[s.c % 2][:, 0:LO], psg[s.c % 2][:, 0:LO], 1.0 / SCALE)

            with if_sorted(dve):
                chunk_loop(dve, body)
                mean(Chunk(0, CH - 1))
                finish_norm(nc, dve, h, f, Chunk(0, CH - 1))

        @block.tensor
        def _(pe):
            def degrees(s, l):
                n = (s.c * AL + l) % 2
                pe.wait_ge(two_ready, s.times(AL, l + 1))
                for k in range(2):
                    last = nc.tensor.matmul(psg[s.c % 2][:, 0:LO], h.ones16[:], two[n][:, k], start=(l == 0 and k == 0),
                                            stop=(l == AL - 1 and k == 1))
                last.then_inc(deg_done, 1)

            def body(s, half):
                reach(pe, f.mean_ready, s.times(1, -1))
                for l in range(AL):
                    pe.wait_ge(a_in[l], s.times(16, 16))
                    for w in range(AW):
                        for part in range(2):
                            last = nc.tensor.matmul(psx[s.c % 2][:, 0:LO], h.x1s[:, l * AW + w, part, :], a[l][:, w],
                                                    start=(l == 0 and w == 0 and part == 0),
                                                    stop=(l == AL - 1 and w == AW - 1 and part == 1))
                    last.then_inc(a_used, 1)
                    if l == 0 and s.c >= 1:
                        degrees(s.back(1), AL - 1)
                    if l >= 1:
                        degrees(s, l - 1)
                    if l == 2 and s.c >= 1:
                        finish_product(nc, pe, h, f, s.back(1))

            with if_sorted(pe):
                chunk_loop(pe, body)
                degrees(Chunk(0, CH - 1), AL - 1)
                finish_product(nc, pe, h, f, Chunk(0, CH - 1))


def build(nc, given):
    with ExitStack() as ctx:
        m = Place(nc, ctx)
        h = Shared()
        h.xT, h.x_tiles, h.xT_tiles = given["xT"], given["x_tiles"], given["xT_tiles"]
        h.src_keys, h.dst_keys, h.dst_col = given["src_keys"], given["dst_keys"], given["dst_col"]
        h.samples, h.dst_first = given["samples"], given["dst_first"]
        h.src_idx, h.dst_idx, h.ea_blocks = given["src_idx"], given["dst_idx"], given["ea_blocks"]
        h.w1aT, h.w1bT, h.b1, h.w2, h.b2 = given["w1aT"], given["w1bT"], given["b1"], given["w2"], given["b2"]
        h.wihT, h.bih, h.whhT, h.bhh = given["wihT"], given["bih"], given["whhT"], given["bhh"]
        h.weight_in, h.root_in, h.bias_in = given["weight_in"], given["root_in"], given["bias_in"]
        h.out = given["out"]

        def dram(name, shape, dt=fp32):
            return nc.dram_tensor(name, shape, dt, kind="Internal").ap()

        h.y = dram("y", (NP, D))
        h.y_rows = h.y.rearrange("(k p j) d -> k p j d", p=P, j=WB)
        h.A = [dram(f"A{k}", (P // 2, GP * LO), fp16) for k in range(2)]
        h.first_group = dram("first_group", (1, GP), int32)
        h.first_of = h.first_group.rearrange("a (w p) -> (a w) p", p=P // GN)
        h.deg = dram("deg", (1, NP))
        h.x1, h.r = dram("x1", (NP, D)), dram("r", (NP, D))

        h.agg = m.sb("agg", [P, NP])
        h.w1b = m.sb("w1b", [P, D])
        h.wih, h.whh, h.wc = m.sb("wih", [D, 3 * D]), m.sb("whh", [D, 3 * D]), m.sb("wc", [D, 3 * D])
        h.weight, h.root = m.sb("weight", [D, D]), m.sb("root", [D, D])
        h.bias4, h.bias2 = m.sb("bias4", [1, 4 * D]), m.sb("bias2", [2, 4 * D])
        h.ident, h.ones, h.ones16 = m.sb("ident", [P, P]), m.sb("ones", [P, P]), m.sb("ones16", [P, P], fp16)
        h.caught, h.sorted = m.sb("caught", [P, 1]), m.sb("sorted", [1, 1], int32)
        h.rowsum = m.sb("rowsum", [P, GP], fp16)
        h.iota_lo = m.sb("iota_lo", [P, LO], fp16)
        h.iota_key = m.sb("iota_key", [P, P], fp16)
        h.weights = [(h.w1b[0:DE], h.w1bT), (h.wih[:], h.wihT), (h.whh[:], h.whhT), (h.weight[:], h.weight_in),
                     (h.root[:], h.root_in)] + [(h.bias4[:, k * D:(k + 1) * D], h.bias_in) for k in range(4)]
        with ExitStack() as keys:
            k = Place(nc, keys)
            h.key1, h.key2 = k.sb("key1", [P, KWP]), k.sb("key2", [P, KWP], fp16)
            h.seg_key = k.sb("seg_key", [P, TILES], fp16)
            prologue(nc, h)
            edges(nc, h)
        verdict(nc, h)
        general(nc, h, 0)
        h.x1s = h.agg[:].bitcast(fp16).rearrange("p (w h d) -> p w h d", h=2, d=D)
        with ExitStack() as rows:
            k = Place(nc, rows)
            h.v, h.mv = k.sb("v", [P, W, D]), k.sb("mv", [P, W, 2])
            gates(nc, h)
            normalise(nc, h)
        sources(nc, h)
        general(nc, h, 1)


def windows(edge_rows, pad):
    import numpy as np
    flat = np.full(STEP * (KWP - 1) + P, pad, edge_rows.dtype)
    flat[:EDGES] = edge_rows
    return np.stack([flat[p:p + STEP * KWP - STEP + 1:STEP] for p in range(P)])


def layouts(x, src, dst, edge_attr_64, L0_gnn_W1, L0_gnn_b1, L0_gnn_W2, L0_gnn_b2, L0_gnn_Wih, L0_gnn_bih, L0_gnn_Whh,
            L0_gnn_bhh, L1_gnn_weight, L1_gnn_root_weight, L1_gnn_bias):
    import numpy as np
    padded = np.zeros((NP, D), x.dtype)
    padded[:NODES] = x
    tiles = padded.reshape(GR, W, GN, D).transpose(2, 0, 1, 3).reshape(P, W, D)

    def new_first(t):
        return np.concatenate([t[2 * D:], t[:2 * D]])

    return dict(
        xT=padded.T, x_tiles=tiles.reshape(P, W * D), xT_tiles=tiles.transpose(2, 1, 0).reshape(D, W * P),
        src_keys=windows(src, 0), dst_keys=windows(dst, NOEDGE), dst_col=dst.reshape(TILES, P).T,
        samples=dst[::STEP].reshape(SR, SAMP), dst_first=dst[::BE][None],
        src_idx=src.reshape(BLOCKS, BT, P).transpose(0, 2, 1), dst_idx=dst.reshape(BLOCKS, BT, P).transpose(0, 2, 1),
        ea_blocks=edge_attr_64.reshape(BLOCKS, BE, DE).transpose(0, 2, 1),
        w1aT=L0_gnn_W1[:, :D].T, w1bT=L0_gnn_W1[:, D:].T, b1=L0_gnn_b1, w2=L0_gnn_W2, b2=L0_gnn_b2[:, None],
        wihT=new_first(L0_gnn_Wih).T, bih=new_first(L0_gnn_bih)[None], whhT=L0_gnn_Whh.T, bhh=L0_gnn_bhh[None],
        weight_in=L1_gnn_weight, root_in=L1_gnn_root_weight, bias_in=L1_gnn_bias[None])


def kernel(**inputs):
    import numpy as np
    import concourse.bacc as bacc
    from concourse.bass_utils import run_bass_kernel_spmd as run

    nc = bacc.Bacc("TRN2", target_bir_lowering=False, num_devices=1)
    arrays, args = {}, {}
    for name, a in layouts(**{k: np.asarray(v) for k, v in inputs.items()}).items():
        arrays[f"in_{name}_dram"] = np.ascontiguousarray(a)
        args[name] = nc.dram_tensor(f"in_{name}_dram", a.shape, mybir.dt.from_np(a.dtype), kind="ExternalInput").ap()
    args["out"] = nc.dram_tensor("out_0_dram", (NP, D), fp32, kind="ExternalOutput").ap()
    build(nc, args)
    r = run(nc, [arrays], core_ids=[0])
    return r.results[0]["out_0_dram"][:NODES]
```
